# Optimizing a Trainium2 kernel written in Bass

```python
import numpy as np
import jax
import jax.numpy as jnp

def _softmax(x, axis=-1):
    return jax.nn.softmax(x, axis=axis)

def _gelu(x):
    return jax.nn.gelu(x, approximate=True)

def _silu(x):
    return jax.nn.silu(x)

def _sigmoid(x):
    return jax.nn.sigmoid(x)

def _layernorm(x, axis=-1, eps=1e-05):
    m = jnp.mean(x, axis=axis, keepdims=True)
    v = jnp.var(x, axis=axis, keepdims=True)
    return (x - m) / jnp.sqrt(v + eps)

def _scatter_add(tgt, idx, src, axis=0):
    return tgt.at[idx].add(src)

def _segment_sum(src, seg, n):
    return jax.ops.segment_sum(src, seg, n)
kernel_name = 'mk_gnn_resnorm_d1_gnn_r8_c26de4'

def setup_inputs(seed: int=0):
    np.random.seed(seed)
    _w = jnp.asarray

    def _rec_inputs():
        import jax
        import jax.numpy as jnp
        _gk = jax.random.key(seed)
        x = -0.000202 + 1 * jax.random.normal(jax.random.fold_in(_gk, 1), (6250, 128), jnp.float32)
        _s = jax.random.randint(jax.random.fold_in(_gk, 2), (100000,), 0, 6250, jnp.int32)
        _d = jax.random.randint(jax.random.fold_in(_gk, 3), (100000,), 0, 6250, jnp.int32)
        _loop = jnp.arange(6250, dtype=jnp.int32)
        src = jnp.concatenate([_s, _d, _loop])
        dst = jnp.concatenate([_d, _s, _loop])
        _o = jnp.argsort(dst, stable=True)
        src = src[_o]
        dst = dst[_o]
        edge_attr_64 = -7.08334e-05 + 0.999895 * jax.random.normal(jax.random.fold_in(_gk, 11), (206250, 64), jnp.float32)
        return (x, src, dst, edge_attr_64)
    x, src, dst, edge_attr_64 = _rec_inputs()

    def _L0_gnn_setup():
        import jax, jax.numpy as jnp
        import numpy as np
        N_NODES = 6250
        N_EDGES = 75000
        HIDDEN = 128
        N_RBF = 64
        key = jax.random.key(seed)
        ks = jax.random.split(key, 12)
        s = 1.0 / np.sqrt(HIDDEN)
        sr = 1.0 / np.sqrt(N_RBF)
        return {'h': jax.random.normal(ks[0], (N_NODES, HIDDEN), dtype=jnp.float32), 'rbf': jax.random.normal(ks[1], (N_EDGES, N_RBF), dtype=jnp.float32), 'edge_index': jax.random.randint(ks[2], (2, N_EDGES), 0, N_NODES, dtype=jnp.int64), 'We1': jax.random.uniform(ks[3], (N_RBF, HIDDEN), jnp.float32, -sr, sr), 'be1': jax.random.uniform(ks[4], (HIDDEN,), jnp.float32, -sr, sr), 'We2': jax.random.uniform(ks[5], (HIDDEN, HIDDEN), jnp.float32, -s, s), 'be2': jax.random.uniform(ks[6], (HIDDEN,), jnp.float32, -s, s), 'Wlin': jax.random.uniform(ks[7], (HIDDEN, HIDDEN), jnp.float32, -s, s), 'Wn1': jax.random.uniform(ks[8], (HIDDEN, HIDDEN), jnp.float32, -s, s), 'bn1': jax.random.uniform(ks[9], (HIDDEN,), jnp.float32, -s, s), 'Wn2': jax.random.uniform(ks[10], (HIDDEN, HIDDEN), jnp.float32, -s, s), 'bn2': jax.random.uniform(ks[11], (HIDDEN,), jnp.float32, -s, s)}
    _L0_gnn_all = _L0_gnn_setup()
    _L0_gnn_in = {k: v for k, v in _L0_gnn_all.items() if k in ('We1', 'be1', 'We2', 'be2', 'Wlin', 'Wn1', 'bn1', 'Wn2', 'bn2')}
    del _L0_gnn_all
    return {'x': x, 'src': src, 'dst': dst, 'edge_attr_64': edge_attr_64, 'L0_gnn_We1': _L0_gnn_in['We1'], 'L0_gnn_be1': _L0_gnn_in['be1'], 'L0_gnn_We2': _L0_gnn_in['We2'], 'L0_gnn_be2': _L0_gnn_in['be2'], 'L0_gnn_Wlin': _L0_gnn_in['Wlin'], 'L0_gnn_Wn1': _L0_gnn_in['Wn1'], 'L0_gnn_bn1': _L0_gnn_in['bn1'], 'L0_gnn_Wn2': _L0_gnn_in['Wn2'], 'L0_gnn_bn2': _L0_gnn_in['bn2']}

def reference(x, src, dst, edge_attr_64, L0_gnn_We1, L0_gnn_be1, L0_gnn_We2, L0_gnn_be2, L0_gnn_Wlin, L0_gnn_Wn1, L0_gnn_bn1, L0_gnn_Wn2, L0_gnn_bn2):
    import jax
    import jax.numpy as jnp

    def _L0_gnn_ref(h, rbf, edge_index, We1, be1, We2, be2, Wlin, Wn1, bn1, Wn2, bn2):
        import jax, jax.numpy as jnp
        import numpy as np
        N_NODES = 6250
        N_EDGES = 75000
        HIDDEN = 128
        N_RBF = 64
        src, dst = (edge_index[0], edge_index[1])
        w = jax.nn.silu(rbf @ We1 + be1) @ We2 + be2
        m = w * (h[src] @ Wlin)
        agg = jax.ops.segment_sum(m, dst, num_segments=h.shape[0])
        out = jax.nn.silu(agg @ Wn1 + bn1) @ Wn2 + bn2
        return h + out
    edge_index = jnp.stack([src, dst])
    x = _layernorm(x + _L0_gnn_ref(x, edge_attr_64, edge_index, L0_gnn_We1, L0_gnn_be1, L0_gnn_We2, L0_gnn_be2, L0_gnn_Wlin, L0_gnn_Wn1, L0_gnn_bn1, L0_gnn_Wn2, L0_gnn_bn2), axis=-1)
    return x

_drawn_inputs = setup_inputs


def setup_inputs(seed=0):
    import zlib

    import numpy as np

    out = dict(_drawn_inputs(seed))
    spreads = {}
    factors = {'L0_gnn_be1': 8.0, 'L0_gnn_be2': 3.746, 'L0_gnn_bn1': 6.283}
    for name, (base, spread) in spreads.items():
        noise = np.random.default_rng([zlib.crc32(name.encode()), seed]).standard_normal(out[name].shape)
        drawn = base * np.exp(spread * noise) if base else spread * noise
        out[name] = jnp.asarray(drawn.astype(out[name].dtype))
    for name, factor in factors.items():
        out[name] = (out[name] * factor).astype(out[name].dtype)
    return out
```

```python
from contextlib import ExitStack

import concourse.bass as bass
from concourse import mybir

P = 128
TILES = 4
SUP = TILES * P
CHUNK = 4
BODY = 8
WIN = 128
ROWS = 4
SPLIT_AT = 3
XLOADS = 7
LN_EPS = 1e-05

ALU = mybir.AluOpType
ACT = mybir.ActivationFunctionType
F32 = mybir.dt.float32
BF16 = mybir.dt.bfloat16
I32 = mybir.dt.int32
AX = mybir.AxisListType


def build_gnn_layer(nc, xT, x_rows, rbfT, srcT, dstT, first_dst,
                    We1, be1, We2, be2, Wlin, Wn1, bn1, Wn2, bn2, out):
    H = P
    NBLK = x_rows.shape[1] // H
    NPAD = P * NBLK
    NSUP = first_dst.shape[1]
    K = rbfT.shape[1] // 2
    LOOPS = NSUP // BODY
    TAIL = NSUP - LOOPS * BODY
    NGRP = -(-NBLK // ROWS)
    GROUPS = [(g * ROWS, min(NBLK, (g + 1) * ROWS)) for g in range(NGRP)]
    AGG_COLS = NPAD - 1 + WIN
    FAR = float(1 << 20)
    NWIN = -(-NPAD // WIN)
    PARTS, done_groups = [], 0
    for it in (LOOPS // 3, 2 * LOOPS // 3, LOOPS - 4):
        passed = (it * BODY + SPLIT_AT) * NPAD // NSUP - WIN
        groups = max(done_groups, passed // (ROWS * P))
        PARTS.append((it, done_groups, groups))
        done_groups = groups
    LAST_PART = (done_groups, NGRP)
    assert PARTS[0][0] > 1 and all(a[0] < b[0] for a, b in zip(PARTS, PARTS[1:]))
    assert all(g1 > g0 for _, g0, g1 in PARTS) and done_groups < NGRP
    assert K * 2 == P and LOOPS >= 2 and TAIL < CHUNK and BODY == 2 * CHUNK

    WEIGHT_LOADS = 7

    hl_table = nc.dram_tensor("hl_table", (NPAD, H), F32, kind="Internal").ap()

    ctx = ExitStack()
    with ctx:
        def sb(name, shape, dt):
            return ctx.enter_context(nc.sbuf_tensor(name, shape, dt))

        def sem(name):
            return ctx.enter_context(nc.semaphore(name))

        xT_h2T = sb("xT_h2T", [P, NPAD], F32)
        hl_y = sb("hl_y", [P, NBLK * H], F32)
        x_sb = sb("x_sb", [P, NBLK * H], F32)
        aggT = sb("aggT", [P, AGG_COLS], F32)
        rbf_sb = sb("rbf_sb", [P, 2, 2 * SUP], F32)
        idx_sb = sb("idx_sb", [P, 2, CHUNK * TILES], I32)
        hl_src = sb("hl_src", [P, BODY, TILES * H], F32)
        h1_sb = sb("h1_sb", [P, 2, SUP], F32)
        msg_sb = sb("msg_sb", [P, 2, TILES * H], F32)
        onehot = sb("onehot", [P, 2, TILES * WIN], F32)
        dst_i = sb("dst_i", [P, NSUP * TILES], I32)
        first_bc = sb("first_bc", [P, NSUP], I32)
        rel = sb("rel", [P, NSUP * TILES], F32)
        missed = sb("missed", [P, NSUP * TILES], F32)
        below = sb("below", [P, NSUP * TILES], F32)
        counts = sb("counts", [P, 2 + len(PARTS)], F32)
        any_missed = sb("any_missed", [1, 1], I32)
        none_late = sb("none_late", [1, 1], I32)
        left = sb("left", [P, TILES], F32)
        We1_sb = sb("We1_sb", [P, H], F32)
        We2_sb = sb("We2_sb", [P, H], F32)
        Wlin_sb = sb("Wlin_sb", [P, H], F32)
        Wn1_sb = sb("Wn1_sb", [P, H], F32)
        Wn2_sb = sb("Wn2_sb", [P, H], F32)
        be1_sb = sb("be1_sb", [P, 1], F32)
        bn1_sb = sb("bn1_sb", [P, 1], F32)
        bias3 = sb("bias3", [3, 2, H], F32)
        part3 = sb("part3", [3, 3, 2, H], BF16)
        rest3 = sb("rest3", [3, 2, 2, H], F32)
        diff3 = sb("diff3", [3, 3], I32)
        eye3 = sb("eye3", [3, 3], F32)
        mix3 = sb("mix3", [3, 2, 2, H], F32)
        split_rows = sb("split_rows", [3, 2, ROWS * H], BF16)
        ones3 = sb("ones3", [3, P], BF16)
        ones_col = sb("ones_col", [P, 1], F32)
        iota_i = sb("iota_i", [P, WIN], I32)
        stats = sb("stats", [P, NBLK, 6], F32)
        mean_var = sb("mean_var", [P, NBLK, 2], F32)
        std = sb("std", [P, NBLK], F32)
        rstd = sb("rstd", [P, NBLK], F32)
        shift = sb("shift", [P, NBLK], F32)

        def bank(name):
            return ctx.enter_context(nc.psum_tensor(name, [P, 512], F32))

        h1_ps = bank("h1_ps")
        w_ps = [bank("w_ps0"), bank("w_ps1")]
        agg_ps = [bank("agg_ps0")[:, 0:WIN], bank("agg_ps1")[:, 0:WIN]]
        node_ps = [bank("node_ps0"), bank("node_ps1")]
        const_ps = bank("const_ps")
        iota_ps = const_ps[:, 0:WIN]
        count_ps = const_ps[:, WIN:WIN + 2]
        four_banks = [h1_ps] + w_ps + node_ps[0:1]

        xT_loaded = [sem(f"xT_loaded{i}") for i in range(XLOADS)]
        wlin_loaded = sem("wlin_loaded")
        weights_loaded = sem("weights_loaded")
        biases_loaded = sem("biases_loaded")
        dst_loaded = sem("dst_loaded")
        x_loaded = sem("x_loaded")
        consts_made = sem("consts_made")
        chain = sem("chain")
        hl_ready = sem("hl_ready")
        hl_out_act = sem("hl_out_act")
        hl_out_dve = sem("hl_out_dve")
        table_stored = sem("table_stored")
        split_ready = sem("split_ready")
        iota_ready = sem("iota_ready")
        missed_counted = sem("missed_counted")
        missed_summed = sem("missed_summed")
        flag_ready = sem("flag_ready")
        rbf_loaded = [sem("rbf_loaded0"), sem("rbf_loaded1")]
        idx_loaded = [sem("idx_loaded0"), sem("idx_loaded1")]
        gathered = [sem(f"gathered{i}") for i in range(BODY)]
        h1_ready = sem("h1_ready")
        silu_done = sem("silu_done")
        w_ready = sem("w_ready")
        onehot_ready = sem("onehot_ready")
        msg_ready = sem("msg_ready")
        agg_ready = sem("agg_ready")
        added = sem("added")
        p2_rbf = sem("p2_rbf")
        p2_idx = sem("p2_idx")
        p2_gathered = sem("p2_gathered")
        p2_h1 = sem("p2_h1")
        p2_silu = sem("p2_silu")
        p2_w = sem("p2_w")
        p2_msg = sem("p2_msg")
        p2_onehot = sem("p2_onehot")
        p2_agg = sem("p2_agg")
        p2_added = sem("p2_added")
        p2_moved = sem("p2_moved")
        p2_set = sem("p2_set")
        pass2_done = sem("pass2_done")
        o1_ready = sem("o1_ready")
        h2_ready = sem("h2_ready")
        o2_ready = sem("o2_ready")
        y_ready = sem("y_ready")
        stats_ready = sem("stats_ready")
        mv_ready = sem("mv_ready")
        var_ready = sem("var_ready")
        std_ready = sem("std_ready")
        ln_ready = sem("ln_ready")
        normed_dve = sem("normed_dve")
        normed_act = sem("normed_act")
        out_stored = sem("out_stored")

        def nth(it, j):
            return it * BODY + j

        def turn(it, j, period):
            return it * (BODY // period) + j // period + 1

        def rbf_of(j):
            slot, half, pair = (j // CHUNK) % 2, j % 2, (j % CHUNK) // 2
            return rbf_sb[half * K:(half + 1) * K, slot, pair * SUP:(pair + 1) * SUP]

        def at_first(it, j, n):
            return isinstance(it, int) and it == 0 and j < n

        def run(eng, step, nodes=None, after=SPLIT_AT):
            splits = [it for it, _, _ in PARTS] if nodes else []
            for n, it in enumerate([0] + splits):
                for j in range(BODY):
                    step(it, j)
                    if n and j == after:
                        nodes(n - 1)
                end = (splits + [LOOPS])[n]
                if end - it == 2:
                    for j in range(BODY):
                        step(it + 1, j)
                elif end - it > 2:
                    with eng.Fori(it + 1, end) as i:
                        for j in range(BODY):
                            step(i, j)
            for j in range(TAIL):
                step(LOOPS, j)

        def run_second(eng, step):
            with eng.Fori(0, NSUP // CHUNK) as c:
                for j in range(CHUNK):
                    step(c, j)
            for j in range(NSUP % CHUNK):
                step(NSUP // CHUNK, j)

        def if_missed(eng, body):
            eng.wait_ge(flag_ready, 2)
            flag = eng.value_load(any_missed[0:1, 0:1], min_val=0, max_val=1)
            with eng.If(flag > 0):
                body()

        def if_late(eng, late, body):
            eng.wait_ge(flag_ready, 2)
            flag = eng.value_load(none_late[0:1, 0:1], min_val=0, max_val=1)
            with eng.If(flag < 1 if late else flag > 0):
                body()

        def nodes_of(eng, part):
            def early(n):
                if_late(eng, False, lambda: part(n, PARTS[n][1], PARTS[n][2], PARTS[n][0] * BODY + SPLIT_AT))

            def rest():
                def both():
                    for n, (_, g0, g1) in enumerate(PARTS):
                        part(n, g0, g1, None)
                if_late(eng, True, both)
                part(len(PARTS), *LAST_PART, None)
            return early, rest

        block = ctx.enter_context(nc.Block())

        @block.sync
        def _(sp):
            per = -(-NBLK // XLOADS)
            for i in range(XLOADS):
                a, b = i * per * P, min(NBLK, (i + 1) * per) * P
                sp.dma_start(xT_h2T[:, a:b], xT[:, a:b]).then_inc(xT_loaded[i], 16)

            def load_chunk(c, slot):
                sp.dma_start(idx_sb[:, slot, :], srcT[c, :, :]).then_inc(idx_loaded[slot], 16)
                sp.dma_start(rbf_sb[:, slot, :], rbfT[c, :, :]).then_inc(rbf_loaded[slot], 16)

            table = hl_table.rearrange("(p b) h -> p (b h)", p=P)
            for g, (b0, b1) in enumerate(GROUPS):
                sp.wait_ge(hl_out_act if g % 2 == 0 else hl_out_dve, g // 2 + 1)
                sp.dma_start(table[:, b0 * H:b1 * H], hl_y[:, b0 * H:b1 * H]).then_inc(table_stored, 16)

            load_chunk(0, 0)
            sp.dma_start(dst_i[:, :], dstT).then_inc(dst_loaded, 16)
            sp.dma_start(first_bc[:, :], first_dst.partition_broadcast(P)).then_inc(dst_loaded, 16)
            for k, b in enumerate((be2, bn2)):
                sp.dma_start(bias3[:, k, :], b.rearrange("(a h) -> a h", a=1).partition_broadcast(3))\
                   .then_inc(biases_loaded, 16)
            for half in range(2):
                sp.dma_start(We1_sb[half * K:(half + 1) * K, :], We1).then_inc(weights_loaded, 16)
            for w_sb, w in ((We2_sb, We2), (Wn1_sb, Wn1), (Wn2_sb, Wn2)):
                sp.dma_start(w_sb[:, :], w).then_inc(weights_loaded, 16)
            for b_sb, b in ((be1_sb, be1), (bn1_sb, bn1)):
                sp.dma_start(b_sb[:, :], b.rearrange("(h a) -> h a", a=1)).then_inc(weights_loaded, 16)
            load_chunk(1, 1)
            sp.dma_start(x_sb[:, :], x_rows).then_inc(x_loaded, 16)

            def next_chunk(it, half):
                c = it * 2 + half
                for j in range(CHUNK):
                    sp.wait_ge(gathered[half * CHUNK + j], it * (16 * TILES))
                sp.wait_ge(h1_ready, c * CHUNK - CHUNK)
                load_chunk(c, half)

            with sp.Fori(1, LOOPS) as it:
                next_chunk(it, 0)
                next_chunk(it, 1)
            if TAIL:
                next_chunk(LOOPS, 0)

            def second():
                sp.wait_ge(added, NSUP)

                def step(c, j):
                    half, pair = j % 2, j // 2
                    sp.wait_ge(p2_msg, c * CHUNK + j + 1)
                    sp.dma_start(idx_sb[:, 0, 0:TILES],
                                 srcT[c, :, j * TILES:(j + 1) * TILES]).then_inc(p2_idx, 16)
                    sp.dma_start(rbf_sb[half * K:(half + 1) * K, 0, 0:SUP],
                                 rbfT[c, half * K:(half + 1) * K, pair * SUP:(pair + 1) * SUP]).then_inc(p2_rbf, 16)
                run_second(sp, step)
            if_missed(sp, second)

        @block.gpsimd
        def _(pool):
            pool.iota(iota_i[:, :], [[1, WIN]], base=0, channel_multiplier=0).then_inc(consts_made, 1)
            pool.iota(diff3[:, :], [[1, 3]], base=0, channel_multiplier=-1).then_inc(consts_made, 1)
            pool.memset(aggT[:, :], 0.0).then_inc(consts_made, 1)
            pool.wait_ge(table_stored, 16 * NGRP)

            rows_used = pool.alloc_register("rows_used")
            pool.reg_mov(rows_used, 0)
            loads2 = pool.alloc_register("loads2")
            pool.reg_mov(loads2, 0)

            def gather(slot_tile, out_slot, t, done):
                pool.indirect_dma_start(
                    hl_src[:, out_slot, t * H:(t + 1) * H], None, hl_table[:, :],
                    bass.IndirectOffsetOnAxis(ap=slot_tile, axis=0)).then_inc(done, 16)

            def step(it, j):
                slot = (j // CHUNK) % 2
                if j % CHUNK == 0:
                    pool.wait_ge(idx_loaded[slot], turn(it, j, BODY) * 16)
                if not at_first(it, j, BODY):
                    pool.reg_add(rows_used, rows_used, 1)
                    pool.wait_ge(table_stored, 16 * NGRP)
                    pool.wait_ge(msg_ready, rows_used)
                for t in range(TILES):
                    col = (j % CHUNK) * TILES + t
                    gather(idx_sb[:, slot, col:col + 1], j, t, gathered[j])
            run(pool, step)

            def second():
                def step2(c, j):
                    pool.reg_add(loads2, loads2, 16)
                    pool.wait_ge(table_stored, 16 * NGRP)
                    pool.wait_ge(p2_idx, loads2)
                    for t in range(TILES):
                        gather(idx_sb[:, 0, t:t + 1], 0, t, p2_gathered)
                run_second(pool, step2)
            if_missed(pool, second)

        @block.scalar
        def _(act):
            act.dma_start(Wlin_sb[:, :], Wlin).then_inc(wlin_loaded, 16)
            for g in range(0, NGRP, 2):
                b0, b1 = GROUPS[g]
                act.wait_ge(hl_ready, g + 1)
                act.activation(hl_y[:, b0 * H:b1 * H], four_banks[g % 4][:, 0:(b1 - b0) * H],
                               ACT.Copy).then_inc(hl_out_act, 1)
            act.wait_ge(weights_loaded, 16 * WEIGHT_LOADS)

            def step(it, j):
                act.wait_ge(h1_ready, nth(it, j) + 1)
                if not at_first(it, j, 2):
                    act.wait_ge(w_ready, nth(it, j) - 1)
                act.activation(h1_sb[:, j % 2, :], h1_ps[:, :], ACT.Silu,
                               bias=be1_sb[:, 0:1]).then_inc(silu_done, 1)

            def part(n, g0, g1, _):
                for g in range(g0, g1):
                    b0, b1 = GROUPS[g]
                    act.wait_ge(o1_ready, g + 1)
                    act.activation(xT_h2T[:, b0 * P:b1 * P], node_ps[g % 2][:, 0:(b1 - b0) * P], ACT.Silu,
                                   bias=bn1_sb[:, 0:1]).then_inc(h2_ready, 1)
                b0, b1 = GROUPS[g0][0], GROUPS[g1 - 1][1]
                act.wait_ge(var_ready, n + 1)
                act.activation(std[:, b0:b1], std[:, b0:b1], ACT.Sqrt).then_inc(std_ready, 1)
                act.wait_ge(ln_ready, 2 * (n + 1))
                for b in range((b0 + b1) // 2, b1):
                    row = hl_y[:, b * H:(b + 1) * H]
                    last = act.activation(row, row, ACT.Identity, bias=shift[:, b:b + 1],
                                          scale=rstd[:, b:b + 1])
                last.then_inc(normed_act, 1)
                for done, c0, c1 in ((normed_dve, b0, (b0 + b1) // 2), (normed_act, (b0 + b1) // 2, b1)):
                    act.wait_ge(done, n + 1)
                    act.dma_start(out[:, c0 * H:c1 * H], hl_y[:, c0 * H:c1 * H]).then_inc(out_stored, 16)

            early, rest = nodes_of(act, part)
            run(act, step, early, SPLIT_AT + 2)

            def second():
                def step2(c, j):
                    act.wait_ge(p2_h1, c * CHUNK + j + 1)
                    act.activation(h1_sb[:, 0, :], h1_ps[:, :], ACT.Silu,
                                   bias=be1_sb[:, 0:1]).then_inc(p2_silu, 1)
                run_second(act, step2)
            if_missed(act, second)
            rest()
            act.wait_ge(out_stored, 16 * 2 * (len(PARTS) + 1))

        @block.tensor
        def _(pe):
            per = -(-NBLK // XLOADS)
            pe.wait_ge(wlin_loaded, 16)
            for g, (b0, b1) in enumerate(GROUPS):
                if g >= 4:
                    pe.wait_ge(hl_out_act if g % 2 == 0 else hl_out_dve, g // 2 - 1)
                for b in range(b0, b1):
                    if b % per == 0:
                        pe.wait_ge(xT_loaded[b // per], 16)
                    last = pe.matmul(four_banks[g % 4][:, (b - b0) * H:(b - b0 + 1) * H],
                                     xT_h2T[:, b * P:(b + 1) * P], Wlin_sb[:, :], start=True, stop=True)
                last.then_inc(hl_ready, 1)
            pe.wait_ge(weights_loaded, 16 * WEIGHT_LOADS)
            pe.wait_ge(split_ready, 3)
            pe.wait_ge(hl_out_act, (NGRP + 1) // 2)
            pe.wait_ge(hl_out_dve, NGRP // 2)

            def with_bias(ps, k, lhsTs, rhs, done):
                n = len(lhsTs)
                pe.matmul(ps[:, 0:n * H], ones3[:, :], split_rows[:, k, 0:n * H], start=True, stop=False)
                for t, lhsT in enumerate(lhsTs):
                    last = pe.matmul(ps[:, t * H:(t + 1) * H], lhsT, rhs, start=False, stop=(t == n - 1))
                last.then_inc(done, 1)

            def first_product(it, j):
                half = j % 2
                if (j % CHUNK) == 0:
                    pe.wait_ge(rbf_loaded[(j // CHUNK) % 2], turn(it, j, BODY) * 16)
                if not at_first(it, j, 1):
                    pe.wait_ge(silu_done, nth(it, j))
                pe.matmul(h1_ps[:, :], We1_sb[half * K:(half + 1) * K, :], rbf_of(j),
                          start=True, stop=True).then_inc(h1_ready, 1)

            def second_product(it, j):
                pe.wait_ge(silu_done, nth(it, j) + 1)
                if not at_first(it, j, 2):
                    pe.wait_ge(msg_ready, nth(it, j) - 1)
                with_bias(w_ps[j % 2], 0, [h1_sb[:, j % 2, t * P:(t + 1) * P] for t in range(TILES)],
                          We2_sb[:, :], w_ready)

            def segment_sum(ps, place, done):
                for t in range(TILES):
                    last = pe.matmul(ps, msg_sb[:, place, t * H:(t + 1) * H],
                                     onehot[:, place, t * WIN:(t + 1) * WIN], start=(t == 0), stop=(t == TILES - 1))
                last.then_inc(done, 1)

            def window_sum(it, j):
                pe.wait_ge(onehot_ready, nth(it, j) + 1)
                pe.wait_ge(msg_ready, nth(it, j) + 1)
                if not at_first(it, j, 2):
                    pe.wait_ge(added, nth(it, j) - 1)
                segment_sum(agg_ps[j % 2], j % 2, agg_ready)

            first_product(0, 0)
            first_product(0, 1)
            second_product(0, 0)

            def step(it, j):
                to_come = TAIL - j if isinstance(it, int) and it == LOOPS else BODY
                if to_come > 2:
                    first_product(it, j + 2)
                if to_come > 1:
                    second_product(it, j + 1)
                window_sum(it, j)
                if at_first(it, j, BODY) and j == BODY - 1:
                    pe.wait_ge(missed_counted, 1)
                    pe.matmul(count_ps[0:1, :], ones_col[:, :], counts[:, 0:2], start=True, stop=True)\
                      .then_inc(missed_summed, 1)

            def part(n, g0, g1, supertiles):
                if supertiles:
                    pe.wait_ge(added, supertiles)
                else:
                    pe.wait_ge(pass2_done, 1)
                for g in range(g0, g1):
                    if g >= g0 + 2:
                        pe.wait_ge(h2_ready, g - 1)
                    elif g0:
                        pe.wait_ge(y_ready, g0)
                    b0, b1 = GROUPS[g]
                    pe.matmul(node_ps[g % 2][:, 0:(b1 - b0) * P], Wn1_sb[:, :], aggT[:, b0 * P:b1 * P],
                              start=True, stop=True).then_inc(o1_ready, 1)
                pe.wait_ge(h2_ready, g1)
                for g in range(g0, g1):
                    if g >= g0 + 2:
                        pe.wait_ge(y_ready, g - 1)
                    with_bias(node_ps[g % 2], 1, [xT_h2T[:, b * P:(b + 1) * P] for b in range(*GROUPS[g])],
                              Wn2_sb[:, :], o2_ready)

            early, rest = nodes_of(pe, part)
            run(pe, step, early)

            def second():
                def step2(c, j):
                    half, n = j % 2, c * CHUNK + j
                    pe.wait_ge(p2_rbf, (n + 1) * 16)
                    pe.matmul(h1_ps[:, :], We1_sb[half * K:(half + 1) * K, :],
                              rbf_sb[half * K:(half + 1) * K, 0, 0:SUP], start=True, stop=True).then_inc(p2_h1, 1)
                    pe.wait_ge(p2_silu, n + 1)
                    with_bias(w_ps[0], 0, [h1_sb[:, 0, t * P:(t + 1) * P] for t in range(TILES)], We2_sb[:, :], p2_w)
                    with pe.Fori(0, NWIN) as v:
                        pe.wait_ge(p2_msg, n + 2)
                        pe.wait_ge(p2_onehot, n * NWIN + v + 1)
                        segment_sum(agg_ps[0], 0, p2_agg)
                run_second(pe, step2)
            if_missed(pe, second)
            rest()

        @block.vector
        def _(dve):
            links = [0]

            def link(ins):
                links[0] += 1
                ins.then_inc(chain, 1)
                dve.wait_ge(chain, links[0])

            for g in range(1, NGRP, 2):
                b0, b1 = GROUPS[g]
                dve.wait_ge(hl_ready, g + 1)
                dve.tensor_copy(hl_y[:, b0 * H:b1 * H], four_banks[g % 4][:, 0:(b1 - b0) * H]).then_inc(hl_out_dve, 1)
            dve.memset(ones_col[:, :], 1.0)
            dve.memset(ones3[:, :], 1.0).then_inc(split_ready, 1)
            dve.wait_ge(consts_made, 3)
            dve.tensor_copy(iota_ps, iota_i[:, :]).then_inc(iota_ready, 1)
            link(dve.tensor_scalar(eye3[:, :], diff3[:, :], 0.0, None, ALU.is_equal))
            dve.wait_ge(biases_loaded, 32)
            link(dve.tensor_copy(part3[:, 0, :, :], bias3[:, :, :]))
            link(dve.tensor_tensor(rest3[:, 0, :, :], bias3[:, :, :], part3[:, 0, :, :], ALU.subtract))
            link(dve.tensor_copy(part3[:, 1, :, :], rest3[:, 0, :, :]))
            link(dve.tensor_tensor(rest3[:, 1, :, :], rest3[:, 0, :, :], part3[:, 1, :, :], ALU.subtract))
            link(dve.tensor_copy(part3[:, 2, :, :], rest3[:, 1, :, :]))
            link(dve.tensor_scalar(mix3[:, 0, :, :], part3[:, 0, :, :], eye3[:, 0:1], None, ALU.mult))
            link(dve.scalar_tensor_tensor(out=mix3[:, 1, :, :], in0=part3[:, 1, :, :], scalar=eye3[:, 1:2],
                                          in1=mix3[:, 0, :, :], op0=ALU.mult, op1=ALU.add))
            for k in range(2):
                rows = split_rows[:, k, :].rearrange("p (t h) -> p t h", t=ROWS)
                dve.scalar_tensor_tensor(
                    out=rows, in0=part3[:, 2, k, :].unsqueeze(1).to_broadcast([3, ROWS, H]), scalar=eye3[:, 2:3],
                    in1=mix3[:, 1, k, :].unsqueeze(1).to_broadcast([3, ROWS, H]),
                    op0=ALU.mult, op1=ALU.add).then_inc(split_ready, 1)

            dve.wait_ge(dst_loaded, 32)
            link(dve.tensor_tensor(rel[:, :].rearrange("p (s t) -> p s t", t=TILES),
                                   dst_i[:, :].rearrange("p (s t) -> p s t", t=TILES),
                                   first_bc[:, :].unsqueeze(2).to_broadcast([P, NSUP, TILES]), ALU.subtract))
            dve.wait_ge(iota_ready, 1)

            iota = iota_ps.unsqueeze(1).to_broadcast([P, TILES, WIN])

            def make_onehot(place, dst_cols, done):
                dve.tensor_tensor(onehot[:, place, :].rearrange("p (t n) -> p t n", t=TILES), iota,
                                  dst_cols.unsqueeze(2).to_broadcast([P, TILES, WIN]), ALU.is_equal).then_inc(done, 1)

            def count_missed():
                link(dve.tensor_scalar(missed[:, :], rel[:, :], 0.0, None, ALU.is_lt))
                link(dve.scalar_tensor_tensor(out=missed[:, :], in0=rel[:, :], scalar=float(WIN), in1=missed[:, :],
                                              op0=ALU.is_ge, op1=ALU.add))
                link(dve.tensor_reduce(counts[:, 1:2], missed[:, :], AX.X, ALU.add))
                for n, (it, _, g1) in enumerate(PARTS):
                    cols = slice((it * BODY + SPLIT_AT) * TILES, NSUP * TILES)
                    link(dve.tensor_scalar(below[:, cols], dst_i[:, cols], float(GROUPS[g1 - 1][1] * P), None,
                                           ALU.is_lt))
                    link(dve.tensor_reduce(counts[:, 2 + n:3 + n], below[:, cols], AX.X, ALU.add))
                dve.tensor_reduce(counts[:, 0:1], counts[:, 1:2 + len(PARTS)], AX.X, ALU.add)\
                   .then_inc(missed_counted, 1)
                dve.wait_ge(missed_summed, 1)
                dve.tensor_scalar(any_missed[:, :], count_ps[0:1, 1:2], 0.0, None, ALU.is_gt)\
                   .then_inc(flag_ready, 1)
                dve.tensor_scalar(none_late[:, :], count_ps[0:1, 0:1], 0.0, None, ALU.is_equal)\
                   .then_inc(flag_ready, 1)

            def step(it, j):
                n, place = nth(it, j), j % 2
                if not at_first(it, j, 2):
                    dve.wait_ge(agg_ready, n - 1)
                make_onehot(place, rel[:, bass.ds(n * TILES, TILES)], onehot_ready)
                dve.wait_ge(w_ready, n + 1)
                dve.wait_ge(gathered[j], turn(it, j, BODY) * 16 * TILES)
                dve.tensor_tensor(msg_sb[:, place, :], w_ps[place][:, :], hl_src[:, j, :],
                                  ALU.mult).then_inc(msg_ready, 1)
                if not at_first(it, j, 1):
                    add_window(n - 1, 1 - place)
                if at_first(it, j, BODY) and j == BODY - 1:
                    count_missed()

            def add_window(n, place):
                start = dve.value_load(first_bc[0:1, bass.ds(n, 1)], min_val=0, max_val=NPAD - 1)
                dve.wait_ge(agg_ready, n + 1)
                if not (isinstance(n, int) and n == 0):
                    dve.wait_ge(added, n)
                cols = aggT[:, bass.ds(start, WIN)]
                dve.tensor_tensor(cols, agg_ps[place], cols, ALU.add).then_inc(added, 1)

            def part(n, g0, g1, _):
                dve.wait_ge(x_loaded, 16)
                for g in range(g0, g1):
                    b0, b1 = GROUPS[g]
                    dve.wait_ge(o2_ready, g + 1)
                    dve.scalar_tensor_tensor(out=hl_y[:, b0 * H:b1 * H], in0=x_sb[:, b0 * H:b1 * H], scalar=2.0,
                                             in1=node_ps[g % 2][:, 0:(b1 - b0) * H],
                                             op0=ALU.mult, op1=ALU.add).then_inc(y_ready, 1)
                    dve.wait_ge(y_ready, g + 1)
                    for b in range(b0, b1):
                        last = dve.bn_stats(stats[:, b, :], hl_y[:, b * H:(b + 1) * H])
                    last.then_inc(stats_ready, 1)
                    dve.wait_ge(stats_ready, g + 1)
                    for b in range(b0, b1):
                        last = dve.bn_aggr(mean_var[:, b, :], stats[:, b, :])
                last.then_inc(mv_ready, 1)
                b0, b1 = GROUPS[g0][0], GROUPS[g1 - 1][1]
                dve.wait_ge(mv_ready, n + 1)
                dve.tensor_scalar(std[:, b0:b1], mean_var[:, b0:b1, 1], LN_EPS, None, ALU.add).then_inc(var_ready, 1)
                dve.wait_ge(std_ready, n + 1)
                dve.reciprocal(rstd[:, b0:b1], std[:, b0:b1]).then_inc(ln_ready, 1)
                dve.wait_ge(ln_ready, 2 * n + 1)
                dve.scalar_tensor_tensor(out=shift[:, b0:b1], in0=mean_var[:, b0:b1, 0], scalar=-1.0,
                                         in1=rstd[:, b0:b1], op0=ALU.mult, op1=ALU.mult).then_inc(ln_ready, 1)
                dve.wait_ge(ln_ready, 2 * n + 2)
                for b in range(b0, (b0 + b1) // 2):
                    row = hl_y[:, b * H:(b + 1) * H]
                    last = dve.tensor_scalar(row, row, rstd[:, b:b + 1], shift[:, b:b + 1], ALU.mult, ALU.add)
                last.then_inc(normed_dve, 1)

            early, rest = nodes_of(dve, part)
            run(dve, step, early)
            add_window(NSUP - 1, (NSUP - 1) % 2)
            dve.wait_ge(added, NSUP)

            def second():
                link(dve.scalar_tensor_tensor(out=rel[:, :], in0=dst_i[:, :], scalar=FAR, in1=missed[:, :],
                                              op0=ALU.add, op1=ALU.mult))
                link(dve.tensor_scalar(rel[:, :], rel[:, :], -FAR, None, ALU.add))
                dve.sem_inc(p2_msg, 1)
                dve.sem_inc(p2_moved, 1)

                def step2(c, j):
                    n = c * CHUNK + j
                    dve.wait_ge(p2_w, n + 1)
                    dve.wait_ge(p2_gathered, (n + 1) * (16 * TILES))
                    dve.tensor_tensor(msg_sb[:, 0, :], w_ps[0][:, :], hl_src[:, 0, :], ALU.mult).then_inc(p2_msg, 1)
                    dve.tensor_copy(left[:, :], rel[:, bass.ds(n * TILES, TILES)]).then_inc(p2_set, 1)
                    with dve.Fori(0, NWIN) as v:
                        m = n * NWIN + v
                        dve.wait_ge(p2_set, n + 1)
                        dve.wait_ge(p2_moved, m + 1)
                        make_onehot(0, left[:, :], p2_onehot)
                        dve.wait_ge(p2_onehot, m + 1)
                        dve.tensor_scalar(left[:, :], left[:, :], float(-WIN), None, ALU.add).then_inc(p2_moved, 1)
                        dve.wait_ge(p2_agg, m + 1)
                        cols = aggT[:, bass.ds(v * WIN, WIN)]
                        dve.tensor_tensor(cols, agg_ps[0], cols, ALU.add).then_inc(p2_added, 1)
                        dve.wait_ge(p2_added, m + 1)
                run_second(dve, step2)
            if_missed(dve, second)
            dve.sem_inc(pass2_done, 1)
            rest()


WEIGHTS = ["We1", "be1", "We2", "be2", "Wlin", "Wn1", "bn1", "Wn2", "bn2"]


def kernel(**inputs):
    import numpy as np
    import concourse.bacc as bacc
    from concourse.bass_utils import run_bass_kernel_spmd

    x, src, dst, rbf = (np.asarray(inputs[k]) for k in ("x", "src", "dst", "edge_attr_64"))
    nodes, hidden = x.shape
    edges, k = rbf.shape
    nblk = -(-nodes // P)
    nsup = -(-edges // SUP)
    nchunk = -(-nsup // CHUNK)
    more = nchunk * CHUNK * SUP - edges

    x_pad = np.concatenate([x, np.zeros((nblk * P - nodes, hidden), x.dtype)])
    assert nblk * P > nodes or edges == nsup * SUP
    src_pad = np.concatenate([src, np.full(more, min(nodes, nblk * P - 1), src.dtype)])
    dst_pad = np.concatenate([dst, np.full(more, dst[-1], dst.dtype)])[:nsup * SUP]
    rbf_pad = np.concatenate([rbf, np.zeros((more, k), rbf.dtype)])

    arrays = {
        "xT": x_pad.reshape(P, nblk, hidden).transpose(2, 1, 0).reshape(hidden, nblk * P),
        "x_rows": x_pad.reshape(nblk, P, hidden).transpose(1, 0, 2).reshape(P, nblk * hidden),
        "rbfT": rbf_pad.reshape(nchunk, CHUNK // 2, 2, SUP, k).transpose(0, 2, 4, 1, 3)
                       .reshape(nchunk, 2 * k, CHUNK // 2 * SUP),
        "srcT": src_pad.reshape(nchunk, CHUNK * TILES, P).transpose(0, 2, 1),
        "dstT": dst_pad.reshape(nsup * TILES, P).T,
        "first_dst": dst_pad[::SUP].reshape(1, nsup),
    }
    for name in WEIGHTS:
        arrays[name] = np.asarray(inputs["L0_gnn_" + name])
    arrays = {f"in_{n}": np.ascontiguousarray(a) for n, a in arrays.items()}

    nc = bacc.Bacc("TRN2", target_bir_lowering=False, num_devices=1)
    args = [nc.dram_tensor(n, a.shape, mybir.dt.from_np(a.dtype), kind="ExternalInput").ap()
            for n, a in arrays.items()]
    out = nc.dram_tensor("out_0", (P, nblk * hidden), F32, kind="ExternalOutput").ap()
    build_gnn_layer(nc, *args, out)
    r = run_bass_kernel_spmd(nc, [arrays], core_ids=[0])
    rows = r.results[0]["out_0"].reshape(P, nblk, hidden).transpose(1, 0, 2).reshape(nblk * P, hidden)
    return np.ascontiguousarray(rows[:nodes])
```
